# Optimizing a Trainium2 kernel written in Bass

```python
import numpy as np
import jax
import jax.numpy as jnp

def _softmax(x, axis=-1):
    return jax.nn.softmax(x, axis=axis)

def _gelu(x):
    return jax.nn.gelu(x, approximate=True)

def _silu(x):
    return jax.nn.silu(x)

def _sigmoid(x):
    return jax.nn.sigmoid(x)

def _layernorm(x, axis=-1, eps=1e-05):
    m = jnp.mean(x, axis=axis, keepdims=True)
    v = jnp.var(x, axis=axis, keepdims=True)
    return (x - m) / jnp.sqrt(v + eps)

def _scatter_add(tgt, idx, src, axis=0):
    return tgt.at[idx].add(src)

def _segment_sum(src, seg, n):
    return jax.ops.segment_sum(src, seg, n)
kernel_name = 'mk_rec_standalone_d1_rec_r8_b08e5a'

def setup_inputs(seed: int=0):
    np.random.seed(seed)
    _w = jnp.asarray

    def _rec_inputs():
        import jax
        import jax.numpy as jnp
        _rk = jax.random.key(seed)
        r_dense_inputs = -0.00338568 + 1.0005 * jax.random.normal(jax.random.fold_in(_rk, 1), (2048, 13), jnp.float32)
        r_sparse_inputs = jnp.stack([jax.random.randint(jax.random.fold_in(jax.random.fold_in(_rk, 2), 0), (2048,), 2, 12500, jnp.int32), jax.random.randint(jax.random.fold_in(jax.random.fold_in(_rk, 2), 1), (2048,), 1, 99999, jnp.int32), jax.random.randint(jax.random.fold_in(jax.random.fold_in(_rk, 2), 2), (2048,), 0, 12500, jnp.int32), jax.random.randint(jax.random.fold_in(jax.random.fold_in(_rk, 2), 3), (2048,), 5, 12500, jnp.int32), jax.random.randint(jax.random.fold_in(jax.random.fold_in(_rk, 2), 4), (2048,), 20, 99993, jnp.int32), jax.random.randint(jax.random.fold_in(jax.random.fold_in(_rk, 2), 5), (2048,), 0, 99993, jnp.int32), jax.random.randint(jax.random.fold_in(jax.random.fold_in(_rk, 2), 6), (2048,), 2, 99999, jnp.int32), jax.random.randint(jax.random.fold_in(jax.random.fold_in(_rk, 2), 7), (2048,), 2, 99995, jnp.int32), jax.random.randint(jax.random.fold_in(jax.random.fold_in(_rk, 2), 8), (2048,), 0, 99999, jnp.int32), jax.random.randint(jax.random.fold_in(jax.random.fold_in(_rk, 2), 9), (2048,), 2, 99986, jnp.int32), jax.random.randint(jax.random.fold_in(jax.random.fold_in(_rk, 2), 10), (2048,), 4, 99999, jnp.int32), jax.random.randint(jax.random.fold_in(jax.random.fold_in(_rk, 2), 11), (2048,), 15, 99999, jnp.int32), jax.random.randint(jax.random.fold_in(jax.random.fold_in(_rk, 2), 12), (2048,), 0, 99989, jnp.int32), jax.random.randint(jax.random.fold_in(jax.random.fold_in(_rk, 2), 13), (2048,), 5, 99990, jnp.int32), jax.random.randint(jax.random.fold_in(jax.random.fold_in(_rk, 2), 14), (2048,), 2, 99996, jnp.int32), jax.random.randint(jax.random.fold_in(jax.random.fold_in(_rk, 2), 15), (2048,), 3, 99994, jnp.int32), jax.random.randint(jax.random.fold_in(jax.random.fold_in(_rk, 2), 16), (2048,), 0, 99998, jnp.int32), jax.random.randint(jax.random.fold_in(jax.random.fold_in(_rk, 2), 17), (2048,), 13, 99998, jnp.int32), jax.random.randint(jax.random.fold_in(jax.random.fold_in(_rk, 2), 18), (2048,), 10, 12498, jnp.int32), jax.random.randint(jax.random.fold_in(jax.random.fold_in(_rk, 2), 19), (2048,), 0, 99999, jnp.int32), jax.random.randint(jax.random.fold_in(jax.random.fold_in(_rk, 2), 20), (2048,), 0, 99995, jnp.int32), jax.random.randint(jax.random.fold_in(jax.random.fold_in(_rk, 2), 21), (2048,), 1, 99998, jnp.int32), jax.random.randint(jax.random.fold_in(jax.random.fold_in(_rk, 2), 22), (2048,), 1, 99997, jnp.int32), jax.random.randint(jax.random.fold_in(jax.random.fold_in(_rk, 2), 23), (2048,), 2, 99989, jnp.int32), jax.random.randint(jax.random.fold_in(jax.random.fold_in(_rk, 2), 24), (2048,), 6, 12500, jnp.int32), jax.random.randint(jax.random.fold_in(jax.random.fold_in(_rk, 2), 25), (2048,), 2, 99995, jnp.int32)], axis=1)
        return (r_dense_inputs, r_sparse_inputs)
    r_dense_inputs, r_sparse_inputs = _rec_inputs()

    def _L0_rec_setup():
        import jax, jax.numpy as jnp
        import numpy as np
        FIELD_NUM = 26
        N_DENSE = 13
        EMBED_DIM = 32
        VOCAB = 12500
        HIDDEN = [256, 128, 64]
        BATCH = 2048
        key = jax.random.key(seed)
        ks = jax.random.split(key, 10)
        u = lambda k, shape, s=0.05: jax.random.uniform(k, shape, jnp.float32, -s, s)
        dense_inputs = jax.random.normal(ks[0], (BATCH, N_DENSE), jnp.float32)
        sparse_inputs = jax.random.randint(ks[1], (BATCH, FIELD_NUM), 0, VOCAB, jnp.int64)
        tables = u(ks[2], (FIELD_NUM, VOCAB, EMBED_DIM))
        w_z = u(ks[3], (FIELD_NUM, EMBED_DIM, HIDDEN[0]))
        w_p = u(ks[4], (FIELD_NUM, FIELD_NUM, HIDDEN[0]))
        l_b = u(ks[5], (HIDDEN[0],))
        W1 = u(ks[6], (HIDDEN[0] + N_DENSE, HIDDEN[1]))
        b1 = jnp.zeros((HIDDEN[1],), jnp.float32)
        Wf = u(ks[7], (HIDDEN[1], 1))
        bf = jnp.zeros((1,), jnp.float32)
        return dict(dense_inputs=dense_inputs, sparse_inputs=sparse_inputs, tables=tables, w_z=w_z, w_p=w_p, l_b=l_b, W1=W1, b1=b1, Wf=Wf, bf=bf)
    _L0_rec_all = _L0_rec_setup()
    _L0_rec_in = {k: v for k, v in _L0_rec_all.items() if k in ('tables', 'w_z', 'w_p', 'l_b', 'W1', 'b1', 'Wf', 'bf')}
    del _L0_rec_all
    return {'r_dense_inputs': r_dense_inputs, 'r_sparse_inputs': r_sparse_inputs, 'L0_rec_tables': _L0_rec_in['tables'], 'L0_rec_w_z': _L0_rec_in['w_z'], 'L0_rec_w_p': _L0_rec_in['w_p'], 'L0_rec_l_b': _L0_rec_in['l_b'], 'L0_rec_W1': _L0_rec_in['W1'], 'L0_rec_b1': _L0_rec_in['b1'], 'L0_rec_Wf': _L0_rec_in['Wf'], 'L0_rec_bf': _L0_rec_in['bf']}

def reference(r_dense_inputs, r_sparse_inputs, L0_rec_tables, L0_rec_w_z, L0_rec_w_p, L0_rec_l_b, L0_rec_W1, L0_rec_b1, L0_rec_Wf, L0_rec_bf):
    import jax
    import jax.numpy as jnp

    def _L0_rec_ref(dense_inputs, sparse_inputs, tables, w_z, w_p, l_b, W1, b1, Wf, bf):
        import jax, jax.numpy as jnp
        import numpy as np
        FIELD_NUM = 26
        N_DENSE = 13
        EMBED_DIM = 32
        VOCAB = 12500
        HIDDEN = [256, 128, 64]
        BATCH = 2048
        embed = tables[jnp.arange(FIELD_NUM)[None, :], sparse_inputs]
        z = embed
        p = jnp.einsum('bfe,bge->bfg', embed, embed)
        l_z = jnp.einsum('bfe,feh->bh', z, w_z)
        l_p = jnp.einsum('bfg,fgh->bh', p, w_p)
        l_1 = jax.nn.relu(jnp.concatenate([l_z + l_p + l_b, dense_inputs], axis=-1))
        h = jax.nn.relu(l_1 @ W1 + b1)
        return jax.nn.sigmoid(h @ Wf + bf)
    y = _L0_rec_ref(r_dense_inputs, r_sparse_inputs, L0_rec_tables, L0_rec_w_z, L0_rec_w_p, L0_rec_l_b, L0_rec_W1, L0_rec_b1, L0_rec_Wf, L0_rec_bf)
    return y

_drawn_inputs = setup_inputs


def setup_inputs(seed=0):
    import zlib

    import numpy as np

    out = dict(_drawn_inputs(seed))
    spreads = {'L0_rec_b1': (0.0, 0.668)}
    factors = {'r_dense_inputs': 7.863,
     'L0_rec_tables': 8.0,
     'L0_rec_w_z': 8.0,
     'L0_rec_w_p': 8.0,
     'L0_rec_l_b': 8.0,
     'L0_rec_W1': 6.393,
     'L0_rec_Wf': 7.371}
    for name, (base, spread) in spreads.items():
        noise = np.random.default_rng([zlib.crc32(name.encode()), seed]).standard_normal(out[name].shape)
        drawn = base * np.exp(spread * noise) if base else spread * noise
        out[name] = jnp.asarray(drawn.astype(out[name].dtype))
    for name, factor in factors.items():
        out[name] = (out[name] * factor).astype(out[name].dtype)
    return out
```

```python
from contextlib import ExitStack

import concourse.bass as bass
from concourse import mybir

F32 = mybir.dt.float32
I32 = mybir.dt.int32
U32 = mybir.dt.uint32
ALU = mybir.AluOpType
ACT = mybir.ActivationFunctionType

P = 128
Q = 32
BANK = 512
DMA = 16


def pnn_kernel(nc, dense, sparse, tables, w_z, w_p, l_b, W1, b1, Wf, bf, out):
    BATCH, NF = sparse.shape
    ND = dense.shape[1]
    _, VOCAB, E = tables.shape
    H = w_z.shape[2]
    H1 = W1.shape[1]
    TILES = BATCH // P
    PER = P // E
    CH = (NF + PER - 1) // PER
    LAST = NF - PER * (CH - 1)
    HALVES = H // P
    QUADS = P // Q
    GROUPS = [(0, 4, 0), (4, CH - 1, 1), (CH - 1, CH, 0)]
    ROWS4 = QUADS
    PER_STEP = 8
    STEPS = P // (ROWS4 * PER_STEP)
    assert E == Q and PER == QUADS and BATCH % (2 * P) == 0 and NF <= Q and ND <= Q and H1 == P

    table_rows = tables.rearrange("f v e -> (f v) e")

    def chunk_fields(j):
        return LAST if j == CH - 1 else PER

    def chunks_with(u):
        return CH if u < LAST else CH - 1

    with ExitStack() as ctx:
        def sb(name, shape, dt=F32):
            return ctx.enter_context(nc.sbuf_tensor(name, shape, dt))

        def ps(name, shape):
            return ctx.enter_context(nc.psum_tensor(name, shape, F32))

        def sem(name):
            return ctx.enter_context(nc.semaphore(name))

        raw = sb("raw", [P, TILES * NF], I32)
        bounded = sb("bounded", [P, TILES * NF])
        wrap = sb("wrap", [P, TILES * NF])
        field_start = sb("field_start", [P, NF], I32)
        ident = sb("ident", [P, P])
        dense_in = sb("dense_in", [P, TILES, Q])
        dense_T = sb("dense_T", [ND, TILES, P])
        wz = sb("wz", [P, CH, H])
        wp = sb("wp", [P, CH, H])
        w1 = sb("w1", [P, HALVES, H1])
        w1_dense = sb("w1_dense", [ND, H1])
        wf = sb("wf", [H1, 1])
        lb_col = sb("lb_col", [P, HALVES])
        b1_col = sb("b1_col", [H1, 1])
        bf_one = sb("bf_one", [1, 1])
        which = sb("which", [P, 2, NF], U32)
        rows = sb("rows", [P, 2, CH * P])
        field_rows = sb("field_rows", [P, CH, P])
        fields = sb("fields", [E, P, Q])
        pairs = sb("pairs", [P, CH, P])
        hidden0 = sb("hidden0", [P, HALVES, P])
        hidden1 = sb("hidden1", [H1, P])
        scores = sb("scores", [1, BATCH])

        ps_turn = ps("ps_turn", [P, 2, BANK])
        ps_prod = ps("ps_prod", [P, 2, PER_STEP * P])
        ps_h0 = ps("ps_h0", [P, HALVES, BANK])
        h0 = [ps_h0[:, h, 0:P] for h in range(HALVES)]
        logit = ps_h0[0:1, 0, P:2 * P]
        h1 = ps_turn[:, 1, 0:P]

        raw_in = sem("raw_in")
        dense_loaded = sem("dense_loaded")
        wz_in = sem("wz_in")
        wp_in = sem("wp_in")
        mlp_in = sem("mlp_in")
        start_made = sem("start_made")
        ident_zero = sem("ident_zero")
        ident_made = sem("ident_made")
        wrap_made = sem("wrap_made")
        bounded_made = sem("bounded_made")
        zeros_made = sem("zeros_made")
        dense_turned = sem("dense_turned")
        dense_made = sem("dense_made")
        which_made = sem("which_made")
        landed = [[sem(f"landed_{s}_{j}") for j in range(CH)] for s in range(2)]
        rows_used = sem("rows_used")
        turned = sem("turned")
        laid_dve = sem("laid_dve")
        laid_act = sem("laid_act")
        prod_made = sem("prod_made")
        moved_dve = sem("moved_dve")
        moved_act = sem("moved_act")
        h0_summed = sem("h0_summed")
        hidden0_dve = sem("hidden0_dve")
        hidden0_act = sem("hidden0_act")
        h1_summed = sem("h1_summed")
        hidden1_made = sem("hidden1_made")
        logit_made = sem("logit_made")
        logit_free = sem("logit_free")
        stored = sem("stored")

        def over_tiles(eng, tile):
            with eng.Fori(0, TILES // 2 - 1) as i:
                for s in range(2):
                    tile(2 * i + s, s, False)
            for s in range(2):
                tile(TILES - 2 + s, s, True)

        def lay(copy, group):
            first, end, bank = GROUPS[group]
            copy(field_rows[:, first:end, :], ps_turn[:, bank, 0:(end - first) * P].rearrange("p (j b) -> p j b", b=P))
            for u in range(PER):
                n = min(end, chunks_with(u)) - first
                if n > 0:
                    src = ps_turn[Q * u:Q * (u + 1), bank, 0:n * P].rearrange("e (j b) -> e b j", b=P)
                    ins = copy(fields[:, :, PER * first + u:PER * (first + n - 1) + u + 1:PER], src)
            return ins

        def move(step, c, k):
            n = chunks_with(k)
            src = ps_prod[Q * c:Q * (c + 1), step % 2, :].rearrange("f (q g) -> f q g", g=P)[
                :, :, NF * c + k:NF * c + k + PER * (n - 1) + 1:PER]
            b0 = step * PER_STEP * ROWS4 + c
            dst = pairs[Q * k:Q * (k + 1), 0:n, b0:b0 + ROWS4 * (PER_STEP - 1) + 1:ROWS4]
            return dst.rearrange("f j q -> f q j"), src

        block = ctx.enter_context(nc.Block())

        @block.sync
        def _(sp):
            sp.dma_start(raw[:, :], sparse.rearrange("(p t) f -> p (t f)", t=TILES)).then_inc(raw_in, DMA)
            sp.wait_ge(zeros_made, 1)
            sp.dma_start(dense_in[:, :, 0:ND], dense.rearrange("(p t) d -> p t d", t=TILES)).then_inc(dense_loaded, DMA)
            wz_rows = w_z.rearrange("f e h -> (f e) h")
            sp.dma_start(wz[:, 0:CH - 1, :], wz_rows[0:(CH - 1) * P, :].rearrange("(j p) h -> p j h", p=P))\
                .then_inc(wz_in, DMA)
            sp.dma_start(wz[0:LAST * E, CH - 1, :], wz_rows[(CH - 1) * P:, :]).then_inc(wz_in, DMA)
            for k in range(PER):
                n = chunks_with(k)
                sp.dma_start(wp[Q * k:Q * k + NF, 0:n, :], w_p[:, k:k + PER * (n - 1) + 1:PER, :]).then_inc(wp_in, DMA)
            sp.dma_start(w1[:, :, :], W1[0:H, :].rearrange("(c p) n -> p c n", p=P)).then_inc(mlp_in, DMA)
            sp.dma_start(w1_dense[:, :], W1[H:H + ND, :]).then_inc(mlp_in, DMA)
            sp.dma_start(wf[:, :], Wf[:, :]).then_inc(mlp_in, DMA)
            with nc.allow_non_contiguous_dma(reason="bias columns, a few hundred values"):
                sp.dma_start(lb_col[:, :], l_b.rearrange("(c p) -> p c", p=P)).then_inc(mlp_in, DMA)
                sp.dma_start(b1_col[:, :], b1.rearrange("(p o) -> p o", o=1)).then_inc(mlp_in, DMA)
            sp.dma_start(bf_one[:, :], bf.rearrange("(p o) -> p o", o=1)).then_inc(mlp_in, DMA)
            sp.wait_ge(logit_free, TILES + 1)
            sp.dma_start(out.rearrange("b o -> o b"), scores[:, :]).then_inc(stored, DMA)
            sp.wait_ge(stored, DMA)

        MLP_LOADS = 6

        @block.gpsimd
        def _(pool):
            nc.gpsimd.iota(field_start[:, :], pattern=[[VOCAB, NF]], base=0, channel_multiplier=0)\
                .then_inc(start_made, 1)
            nc.gpsimd.memset(ident[:, :], 0.0).then_inc(ident_zero, 1)
            pool.wait_ge(ident_zero, 1)
            nc.gpsimd.affine_select(out=ident[:, :], in_=ident[:, :], compare_op=ALU.not_equal, fill=1.0, base=0,
                                    pattern=[[-1, P]], channel_multiplier=1).then_inc(ident_made, 1)

            def gather(t, s, final):
                pool.wait_ge(which_made, t + 1)
                pool.wait_ge(rows_used, t + 1)
                pool.nop(nofuse=True)
                for f in range(NF):
                    nc.gpsimd.indirect_dma_start(
                        rows[:, s, E * f:E * (f + 1)], None, table_rows,
                        bass.IndirectOffsetOnAxis(ap=which[:, s, f:f + 1], axis=0),
                    ).then_inc(landed[s][f // PER], DMA)

            over_tiles(pool, gather)

        @block.vector
        def _(dve):
            nc.vector.memset(dense_in[:, :, :], 0.0)
            nc.vector.memset(wp[:, :, :], 0.0).then_inc(zeros_made, 1)

            dve.wait_ge(raw_in, DMA)
            nc.vector.tensor_scalar(wrap[:, :], raw[:, :], 0.0, float(VOCAB), ALU.is_lt, ALU.mult).then_inc(wrap_made, 1)
            dve.wait_ge(wrap_made, 1)
            nc.vector.scalar_tensor_tensor(out=bounded[:, :], in0=raw[:, :], scalar=float(VOCAB - 1), in1=wrap[:, :],
                                           op0=ALU.min, op1=ALU.add).then_inc(bounded_made, 1)

            def table_index(t, s):
                nc.vector.scalar_tensor_tensor(out=which[:, s, :], in0=bounded[:, bass.ds(t * NF, NF)], scalar=0.0,
                                               in1=field_start[:, :], op0=ALU.max, op1=ALU.add).then_inc(which_made, 1)

            dve.wait_ge(start_made, 1)
            dve.wait_ge(bounded_made, 1)
            table_index(0, 0)
            table_index(1, 1)
            nc.vector.memset(rows[:, :, NF * E:CH * P], 0.0)
            nc.vector.memset(fields[:, :, NF:Q], 0.0).then_inc(zeros_made, 1)
            dve.wait_ge(dense_turned, 1)
            for u in range(QUADS):
                ins = nc.vector.tensor_scalar(dense_T[:, u:TILES:QUADS, :],
                                              ps_turn[Q * u:Q * u + ND, 0, :].rearrange("d (g b) -> d g b", b=P),
                                              0.0, None, ALU.max)
            ins.then_inc(dense_made, 1)
            dve.wait_ge(mlp_in, DMA * MLP_LOADS)

            def tile(t, s, final):
                for group in (0, 2):
                    dve.wait_ge(turned, len(GROUPS) * t + group + 1)
                    lay(nc.vector.tensor_copy, group).then_inc(laid_dve, 1)
                if not final:
                    table_index(t + 2, s)
                for step in range(STEPS):
                    dve.wait_ge(prod_made, STEPS * t + step + 1)
                    for c in range(0, 2):
                        for k in range(PER):
                            ins = nc.vector.tensor_copy(*move(step, c, k))
                    ins.then_inc(moved_dve, 1)
                dve.wait_ge(h0_summed, t + 1)
                nc.vector.tensor_scalar(hidden0[:, 1, :], h0[1], lb_col[:, 1:2], 0.0, ALU.add, ALU.max)\
                    .then_inc(hidden0_dve, 1)
                dve.wait_ge(h1_summed, t + 1)
                nc.vector.tensor_scalar(hidden1[:, :], h1, b1_col[:, 0:1], 0.0, ALU.add, ALU.max)\
                    .then_inc(hidden1_made, 1)

            over_tiles(dve, tile)

        @block.scalar
        def _(act):
            act.wait_ge(mlp_in, DMA * MLP_LOADS)
            act.wait_ge(zeros_made, 2)

            def tile(t, s, final):
                act.wait_ge(turned, len(GROUPS) * t + 2)
                lay(nc.scalar.copy, 1).then_inc(laid_act, 1)
                for step in range(STEPS):
                    act.wait_ge(prod_made, STEPS * t + step + 1)
                    for c in range(2, ROWS4):
                        for k in range(PER):
                            ins = nc.scalar.copy(*move(step, c, k))
                    ins.then_inc(moved_act, 1)
                act.wait_ge(h0_summed, t + 1)
                nc.scalar.activation(hidden0[:, 0, :], h0[0], ACT.Relu, bias=lb_col[:, 0:1]).then_inc(hidden0_act, 1)
                act.wait_ge(logit_made, t + 1)
                nc.scalar.activation(scores[:, :].rearrange("o (b t) -> o t b", t=TILES)[:, bass.ds(t, 1), :],
                                     logit.rearrange("o (t b) -> o t b", t=1), ACT.Sigmoid,
                                     bias=bf_one[:, 0:1]).then_inc(logit_free, 1)

            over_tiles(act, tile)

        @block.tensor
        def _(pe):
            pe.sem_inc(rows_used, 2)
            pe.sem_inc(logit_free, 1)
            pe.wait_ge(ident_made, 1)
            pe.wait_ge(dense_loaded, DMA)
            for g in range(TILES // QUADS):
                ins = nc.tensor.transpose(ps_turn[:, 0, g * P:(g + 1) * P],
                                          dense_in[:, QUADS * g:QUADS * (g + 1), :].rearrange("p t d -> p (t d)"),
                                          ident[:, :])
            ins.then_inc(dense_turned, 1)
            pe.wait_ge(dense_made, 1)
            pe.wait_ge(zeros_made, 2)
            pe.wait_ge(wz_in, DMA * 2)
            pe.wait_ge(wp_in, DMA * PER)
            pe.wait_ge(mlp_in, DMA * MLP_LOADS)

            def turn(t, s, pair, group):
                first, end, bank = GROUPS[group]
                for j in range(first, end):
                    pe.wait_ge(landed[s][j], DMA * chunk_fields(j) * (pair + 1))
                    ins = nc.tensor.transpose(ps_turn[:, bank, (j - first) * P:(j - first + 1) * P],
                                              rows[:, s, j * P:(j + 1) * P], ident[:, :])
                ins.then_inc(turned, 1)

            def linear_term(group):
                first, end, _ = GROUPS[group]
                for j in range(first, end):
                    rows_j = E * chunk_fields(j)
                    for h in range(HALVES):
                        nc.tensor.matmul(h0[h], wz[0:rows_j, j, h * P:(h + 1) * P], field_rows[0:rows_j, j, :],
                                         start=(j == 0), stop=False)

            def tile(t, s, pair):
                turn(t, s, pair, 0)
                turn(t, s, pair, 1)
                pe.wait_ge(laid_dve, 2 * t + 1)
                pe.wait_ge(logit_free, t + 1)
                linear_term(0)
                turn(t, s, pair, 2)
                pe.wait_ge(turned, len(GROUPS) * (t + 1))
                pe.sem_inc(rows_used, 1)
                pe.wait_ge(laid_act, t + 1)
                linear_term(1)
                pe.wait_ge(laid_dve, 2 * t + 2)
                linear_term(2)
                for step in range(STEPS):
                    if step >= 2:
                        pe.wait_ge(moved_dve, STEPS * t + step - 1)
                        pe.wait_ge(moved_act, STEPS * t + step - 1)
                    for q in range(PER_STEP):
                        b0 = ROWS4 * (PER_STEP * step + q)
                        ins = nc.tensor.matmul(ps_prod[:, step % 2, q * P:q * P + ROWS4 * NF],
                                               fields[:, b0:b0 + ROWS4, :].rearrange("e b f -> e (b f)"),
                                               fields[:, b0:b0 + ROWS4, 0:NF], start=True, stop=True)
                    ins.then_inc(prod_made, 1)
                pe.wait_ge(moved_dve, STEPS * (t + 1))
                pe.wait_ge(moved_act, STEPS * (t + 1))
                for j in range(CH):
                    used = Q * chunk_fields(j)
                    for h in range(HALVES):
                        ins = nc.tensor.matmul(h0[h], wp[0:used, j, h * P:(h + 1) * P], pairs[0:used, j, :],
                                               start=False, stop=(j == CH - 1))
                ins.then_inc(h0_summed, 1)
                nc.tensor.matmul(h1, w1_dense[:, :], dense_T[:, bass.ds(t, 1), :].rearrange("d t b -> d (t b)"),
                                 start=True, stop=False)
                pe.wait_ge(hidden0_act, t + 1)
                nc.tensor.matmul(h1, w1[:, 0, :], hidden0[:, 0, :], start=False, stop=False)
                pe.wait_ge(hidden0_dve, t + 1)
                nc.tensor.matmul(h1, w1[:, 1, :], hidden0[:, 1, :], start=False, stop=True).then_inc(h1_summed, 1)
                pe.wait_ge(hidden1_made, t + 1)
                nc.tensor.matmul(logit, wf[:, :], hidden1[:, :], start=True, stop=True).then_inc(logit_made, 1)

            with pe.Fori(0, TILES // 2 - 1) as i:
                for s in range(2):
                    tile(2 * i + s, s, i)
            for s in range(2):
                tile(TILES - 2 + s, s, TILES // 2 - 1)


_INS = ['r_dense_inputs', 'r_sparse_inputs', 'L0_rec_tables', 'L0_rec_w_z', 'L0_rec_w_p', 'L0_rec_l_b', 'L0_rec_W1',
        'L0_rec_b1', 'L0_rec_Wf', 'L0_rec_bf']


def kernel(**inputs):
    import numpy as _np
    import concourse.bacc as _bacc
    from concourse import mybir as _mybir
    from concourse.bass_utils import run_bass_kernel_spmd as _run

    nc = _bacc.Bacc("TRN2", target_bir_lowering=False, num_devices=1)
    arrays, args = {}, []
    for name in _INS:
        a = _np.ascontiguousarray(inputs[name])
        arrays[f"in_{name}"] = a
        args.append(nc.dram_tensor(f"in_{name}", a.shape, _mybir.dt.from_np(a.dtype), kind="ExternalInput").ap())
    batch = inputs['r_dense_inputs'].shape[0]
    args.append(nc.dram_tensor("out_0", (batch, 1), _mybir.dt.float32, kind="ExternalOutput").ap())
    pnn_kernel(nc, *args)
    r = _run(nc, [arrays], core_ids=[0])
    return r.results[0]["out_0"]
```

```python
from contextlib import ExitStack

import concourse.bass as bass
from concourse import mybir

F32 = mybir.dt.float32
I32 = mybir.dt.int32
U32 = mybir.dt.uint32
BF16 = mybir.dt.bfloat16
ALU = mybir.AluOpType
ACT = mybir.ActivationFunctionType
AX = mybir.AxisListType

P = 128
Q = 32
BANK = 512
DMA = 16


def pnn_kernel(nc, dense, sparse, tables, w_z, w_p, l_b, W1, b1, Wf, bf, out):
    BATCH, NF = sparse.shape
    ND = dense.shape[1]
    _, VOCAB, E = tables.shape
    H = w_z.shape[2]
    H1 = W1.shape[1]
    TILES = BATCH // P
    PER = P // E
    CH = (NF + PER - 1) // PER
    LAST = NF - PER * (CH - 1)
    HALVES = H // P
    QUADS = P // Q
    GROUPS = [(0, 2, 0), (2, 4, 1), (4, CH - 1, 1), (CH - 1, CH, 0)]
    GROUP = BANK // P
    NG = TILES // GROUP
    FOUND = LAST
    PARTS = 3
    PICKS = -(-VOCAB // (P * QUADS))
    BLOCKS = QUADS * PICKS
    PU = VOCAB // BLOCKS
    HOTS = (PICKS + 1) // 2
    ROWS4 = QUADS
    PER_STEP = 8
    STEPS = P // (ROWS4 * PER_STEP)
    WARM = [12, 6]
    assert FOUND == 2 and GROUP == 4 and QUADS * PICKS <= 256 and VOCAB % BLOCKS == 0
    assert E == Q and PER == QUADS and BATCH % (2 * P) == 0 and NF <= Q and ND <= Q and H1 == P

    table_rows = tables.rearrange("f v e -> (f v) e")

    def chunk_fields(j):
        return LAST if j == CH - 1 else PER

    def chunks_with(u):
        return CH if u < LAST else CH - 1

    with ExitStack() as ctx:
        def sb(name, shape, dt=F32):
            return ctx.enter_context(nc.sbuf_tensor(name, shape, dt))

        def ps(name, shape):
            return ctx.enter_context(nc.psum_tensor(name, shape, F32))

        def sem(name):
            return ctx.enter_context(nc.semaphore(name))

        raw = sb("raw", [P, TILES * NF], I32)
        bounded = sb("bounded", [P, TILES * NF])
        wrap = sb("wrap", [P, TILES * NF])
        field_start = sb("field_start", [P, NF], I32)
        ident = sb("ident", [P, P])
        dense_in = sb("dense_in", [P, TILES, Q])
        dense_T = sb("dense_T", [ND, TILES, P])
        wz = sb("wz", [P, CH, H])
        wp = sb("wp", [P, CH, H])
        w1 = sb("w1", [P, HALVES, H1])
        w1_dense = sb("w1_dense", [ND, H1])
        wf = sb("wf", [H1, 1])
        lb_col = sb("lb_col", [P, HALVES])
        b1_col = sb("b1_col", [H1, 1])
        bf_one = sb("bf_one", [1, 1])
        which = sb("which", [P, 2, NF], U32)
        rows = sb("rows", [P, 2, CH * P])
        field_rows = sb("field_rows", [P, CH, P])
        fields = sb("fields", [P, P, Q])
        pairs = sb("pairs", [P, CH, P])
        hidden0 = sb("hidden0", [P, HALVES, P])
        hidden1 = sb("hidden1", [H1, P])
        scores = sb("scores", [1, BATCH])
        table_in = sb("table_in", [P, FOUND, BLOCKS * E])
        parts = sb("parts", [P, FOUND, PARTS, BLOCKS * E], BF16)
        look_row = sb("look_row", [P, FOUND, TILES + GROUP])
        ones = sb("ones", [P, P])
        home = sb("home", [P, FOUND, P])
        part_i = sb("part_i", [P, 1], I32)
        before_i = sb("before_i", [P, 1], I32)
        quad_i = sb("quad_i", [P, 1], I32)
        before = sb("before", [P, 1])
        quad_no = sb("quad_no", [P, 1])
        diag = sb("diag", [P, BANK])
        row_i = sb("row_i", [P, BANK], I32)
        c_i = sb("c_i", [P, BANK], I32)
        key = sb("key", [P, BANK], BF16)
        mask = sb("mask", [P, FOUND, BANK])
        hot = sb("hot", [P, 2, HOTS, BANK], BF16)
        picked = sb("picked", [P, FOUND, BANK])
        found = sb("found", [FOUND * E, BANK])

        ps_turn = ps("ps_turn", [P, 2, BANK])
        ps_prod = ps("ps_prod", [P, 2, PER_STEP * P])
        ps_h0 = ps("ps_h0", [P, BANK])
        ps_look = ps("ps_look", [P, BANK])
        h0 = [ps_h0[:, h * P:(h + 1) * P] for h in range(HALVES)]
        logit = ps_h0[0:1, HALVES * P:(HALVES + 1) * P]
        h1 = ps_turn[:, 1, 0:P]

        raw_in = sem("raw_in")
        dense_loaded = sem("dense_loaded")
        wz_in = sem("wz_in")
        wp_in = sem("wp_in")
        mlp_in = sem("mlp_in")
        start_made = sem("start_made")
        ident_zero = sem("ident_zero")
        ident_made = sem("ident_made")
        wrap_made = sem("wrap_made")
        bounded_made = sem("bounded_made")
        zeros_made = sem("zeros_made")
        dense_turned = sem("dense_turned")
        dense_made = sem("dense_made")
        which_made = sem("which_made")
        landed = [[sem(f"landed_{s}_{j}") for j in range(CH)] for s in range(2)]
        rows_used = sem("rows_used")
        turned = sem("turned")
        laid_dve = sem("laid_dve")
        laid_act = sem("laid_act")
        prod_made = sem("prod_made")
        moved_dve = sem("moved_dve")
        moved_act = sem("moved_act")
        h0_summed = sem("h0_summed")
        hidden0_dve = sem("hidden0_dve")
        h1_summed = sem("h1_summed")
        hidden1_made = sem("hidden1_made")
        logit_made = sem("logit_made")
        logit_free = sem("logit_free")
        stored = sem("stored")
        table_loaded = [sem(f"table_loaded_{v}") for v in range(FOUND)]
        part_numbered = sem("part_numbered")
        numbers_made = sem("numbers_made")
        rows_clipped = sem("rows_clipped")
        ones_made = sem("ones_made")
        home_made = sem("home_made")
        part_act = sem("part_act")
        part_dve = sem("part_dve")
        diag_made = sem("diag_made")
        spread = sem("spread")
        spread_read = sem("spread_read")
        row_cut = sem("row_cut")
        keyed = sem("keyed")
        hot_made = sem("hot_made")
        looked = sem("looked")
        masked = sem("masked")
        folded = sem("folded")
        found_made = sem("found_made")

        def over_tiles(eng, tile):
            for q in range(GROUP):
                tile(q, q, 0)
            with eng.Fori(1, NG - 1) as g:
                for q in range(GROUP):
                    tile(GROUP * g + q, q, g)
            for q in range(GROUP):
                tile(GROUP * (NG - 1) + q, q, NG - 1)

        def is_last(t):
            return isinstance(t, int) and t == TILES - 1

        def looks(g):
            return not (isinstance(g, int) and g == NG - 1)

        def has_found(t):
            return not (isinstance(t, int) and t < GROUP)

        def turns(t, group):
            return (len(GROUPS) - 1) * t + GROUP + group + 1 if has_found(t) else len(GROUPS) * t + group + 1

        def last_turned(t):
            return turns(t, len(GROUPS) - 2 if has_found(t) else len(GROUPS) - 1)

        def lay(copy, group, turned_rows=None):
            first, end, bank = GROUPS[group]
            if turned_rows is None:
                turned_rows = ps_turn[:, bank, 0:(end - first) * P]
            used = turned_rows.shape[0]
            copy(field_rows[0:used, first:end, :], turned_rows.rearrange("p (j b) -> p j b", b=P))
            for u in range(PER):
                n = min(end, chunks_with(u)) - first
                if n > 0:
                    src = turned_rows[Q * u:Q * (u + 1), 0:n * P].rearrange("e (j b) -> e b j", b=P)
                    ins = copy(fields[0:E, :, PER * first + u:PER * (first + n - 1) + u + 1:PER], src)
            return ins

        def move(copy, step, rows4):
            b0 = step * PER_STEP * ROWS4
            for c in rows4:
                for k in range(PER):
                    n = chunks_with(k)
                    src = ps_prod[Q * c:Q * (c + 1), step % 2, :].rearrange("f (q g) -> f q g", g=P)[
                        :, :, NF * c + k:NF * c + k + PER * (n - 1) + 1:PER]
                    dst = pairs[Q * k:Q * (k + 1), 0:n, b0 + c:b0 + c + ROWS4 * (PER_STEP - 1) + 1:ROWS4]
                    ins = copy(dst.rearrange("f j q -> f q j"), src)
            return ins

        block = ctx.enter_context(nc.Block())

        @block.sync
        def _(sp):
            sp.dma_start(raw[:, :], sparse.rearrange("(p t) f -> p (t f)", t=TILES)).then_inc(raw_in, DMA)
            sp.wait_ge(zeros_made, 1)
            sp.dma_start(dense_in[:, :, 0:ND], dense.rearrange("(p t) d -> p t d", t=TILES)).then_inc(dense_loaded, DMA)
            wz_rows = w_z.rearrange("f e h -> (f e) h")
            sp.dma_start(wz[:, 0:CH - 1, :], wz_rows[0:(CH - 1) * P, :].rearrange("(j p) h -> p j h", p=P))\
                .then_inc(wz_in, DMA)
            sp.dma_start(wz[0:LAST * E, CH - 1, :], wz_rows[(CH - 1) * P:, :]).then_inc(wz_in, DMA)
            for k in range(PER):
                n = chunks_with(k)
                sp.dma_start(wp[Q * k:Q * k + NF, 0:n, :], w_p[:, k:k + PER * (n - 1) + 1:PER, :]).then_inc(wp_in, DMA)
            sp.dma_start(w1[:, :, :], W1[0:H, :].rearrange("(c p) n -> p c n", p=P)).then_inc(mlp_in, DMA)
            sp.dma_start(w1_dense[:, :], W1[H:H + ND, :]).then_inc(mlp_in, DMA)
            sp.dma_start(wf[:, :], Wf[:, :]).then_inc(mlp_in, DMA)
            with nc.allow_non_contiguous_dma(reason="bias columns, a few hundred values"):
                sp.dma_start(lb_col[:, :], l_b.rearrange("(c p) -> p c", p=P)).then_inc(mlp_in, DMA)
                sp.dma_start(b1_col[:, :], b1.rearrange("(p o) -> p o", o=1)).then_inc(mlp_in, DMA)
            sp.dma_start(bf_one[:, :], bf.rearrange("(p o) -> p o", o=1)).then_inc(mlp_in, DMA)
            HALF = BLOCKS * E // 2
            for v in range(FOUND):
                table = tables[NF - FOUND + v].rearrange("(l r) e -> l (r e)", l=PU)
                for half in range(2):
                    after = FOUND * v + half
                    sp.wait_ge(landed[0][after], DMA * PER)
                    sp.dma_start(table_in[0:PU, v, HALF * half:HALF * (half + 1)],
                                 table[:, HALF * half:HALF * (half + 1)]).then_inc(table_loaded[v], DMA)
            sp.wait_ge(logit_free, TILES + 1)
            sp.dma_start(out.rearrange("b o -> o b"), scores[:, :]).then_inc(stored, DMA)
            sp.wait_ge(stored, DMA)

        MLP_LOADS = 6

        @block.gpsimd
        def _(pool):
            nc.gpsimd.iota(field_start[:, :], pattern=[[VOCAB, NF]], base=0, channel_multiplier=0)\
                .then_inc(start_made, 1)
            nc.gpsimd.iota(part_i[:, :], pattern=[[0, 1]], base=0, channel_multiplier=1)
            nc.gpsimd.iota(before_i[:, :], pattern=[[0, 1]], base=0, channel_multiplier=-BLOCKS).then_inc(part_numbered, 1)
            nc.gpsimd.memset(ident[:, :], 0.0).then_inc(ident_zero, 1)
            pool.wait_ge(ident_zero, 1)
            nc.gpsimd.affine_select(out=ident[:, :], in_=ident[:, :], compare_op=ALU.not_equal, fill=1.0, base=0,
                                    pattern=[[-1, P]], channel_multiplier=1).then_inc(ident_made, 1)

            def gather(t, q, g):
                s = q % 2
                pool.wait_ge(which_made, t + 1)
                pool.wait_ge(rows_used, t + 1)
                pool.nop(nofuse=True)
                for f in range(NF - FOUND if has_found(t) else NF):
                    nc.gpsimd.indirect_dma_start(
                        rows[:, s, E * f:E * (f + 1)], None, table_rows,
                        bass.IndirectOffsetOnAxis(ap=which[:, s, f:f + 1], axis=0),
                    ).then_inc(landed[s][f // PER], DMA)

            over_tiles(pool, gather)

        @block.vector
        def _(dve):
            def bound_indices(tiles):
                cols = slice(NF * tiles[0], NF * tiles[1])
                n = 1 if tiles[0] == 0 else 2
                nc.vector.tensor_scalar(wrap[:, cols], raw[:, cols], 0.0, float(VOCAB), ALU.is_lt, ALU.mult)\
                    .then_inc(wrap_made, 1)
                dve.wait_ge(wrap_made, n)
                nc.vector.scalar_tensor_tensor(out=bounded[:, cols], in0=raw[:, cols], scalar=float(VOCAB - 1),
                                               in1=wrap[:, cols], op0=ALU.min, op1=ALU.add).then_inc(bounded_made, 1)
                dve.wait_ge(bounded_made, n)

            def table_index(t, s):
                nc.vector.scalar_tensor_tensor(out=which[:, s, :], in0=bounded[:, bass.ds(t * NF, NF)], scalar=0.0,
                                               in1=field_start[:, :], op0=ALU.max, op1=ALU.add).then_inc(which_made, 1)

            dve.wait_ge(raw_in, DMA)
            bound_indices((0, 2))
            dve.wait_ge(start_made, 1)
            table_index(0, 0)
            table_index(1, 1)
            nc.vector.memset(dense_in[:, :, :], 0.0)
            nc.vector.memset(wp[:, :, :], 0.0).then_inc(zeros_made, 1)
            bound_indices((2, TILES))
            nc.vector.memset(rows[:, :, NF * E:CH * P], 0.0)
            nc.vector.memset(fields[:, :, :], 0.0).then_inc(zeros_made, 1)
            dve.wait_ge(dense_turned, 1)
            for u in range(QUADS):
                ins = nc.vector.tensor_scalar(dense_T[:, u:TILES:QUADS, :],
                                              ps_turn[Q * u:Q * u + ND, 0, :].rearrange("d (g b) -> d g b", b=P),
                                              0.0, None, ALU.max)
            ins.then_inc(dense_made, 1)
            dve.wait_ge(part_numbered, 1)
            nc.vector.tensor_copy(before[:, :], before_i[:, :])
            nc.vector.tensor_scalar(quad_i[:, :], part_i[:, :], 5, None, ALU.logical_shift_right).then_inc(numbers_made, 1)
            dve.wait_ge(numbers_made, 1)
            nc.vector.tensor_copy(quad_no[:, :], quad_i[:, :]).then_inc(numbers_made, 1)
            nc.vector.memset(look_row[:, :, TILES:TILES + GROUP], 0.0)
            nc.vector.tensor_scalar(look_row[:, :, 0:TILES],
                                    bounded[:, :].rearrange("p (t f) -> p f t", f=NF)[:, NF - FOUND:NF, :],
                                    0.0, None, ALU.max).then_inc(rows_clipped, 1)
            nc.vector.memset(ones[:, :], 1.0).then_inc(ones_made, 1)
            nc.vector.memset(home[:, :, :], 0.0).then_inc(home_made, 1)
            dve.wait_ge(ident_made, 1)
            dve.wait_ge(home_made, 1)
            for v in range(FOUND):
                ins = nc.vector.tensor_reduce(home[:, v, E * v:E * (v + 1)],
                                              ident[:, :].rearrange("p (c e) -> p e c", c=QUADS), AX.X, ALU.add)
            ins.then_inc(home_made, 1)

            def split(v, part):
                dve.wait_ge(part_act, (PARTS - 1) * v + part)
                rest = table_in[0:PU, v, :] if part < PARTS - 1 else parts[0:PU, v, part, :]
                nc.vector.tensor_tensor(rest, table_in[0:PU, v, :], parts[0:PU, v, part - 1, :], ALU.subtract)\
                    .then_inc(part_dve, 1)

            dve.wait_ge(rows_clipped, 1)
            dve.wait_ge(numbers_made, 2)

            def keys(v, target, unit):
                for k in range(GROUP):
                    ins = nc.vector.tensor_scalar(diag[:, k * P:(k + 1) * P], ident[:, :],
                                                  look_row[:, v, bass.ds(target + k, 1)], None, ALU.mult)
                ins.then_inc(diag_made, 1)
                dve.wait_ge(spread, unit + 1)
                nc.vector.tensor_copy(row_i[:, :], ps_prod[:, 0, 0:BANK]).then_inc(spread_read, 1)
                dve.wait_ge(spread_read, unit + 1)
                nc.vector.tensor_scalar(c_i[:, :], row_i[:, :], QUADS - 1, None, ALU.bitwise_and).then_inc(row_cut, 1)
                dve.wait_ge(row_cut, unit + 1)
                nc.vector.scalar_tensor_tensor(out=key[0:PU, :], in0=row_i[0:PU, :], scalar=before[0:PU, 0:1],
                                               in1=c_i[0:PU, :], op0=ALU.add, op1=ALU.subtract)
                nc.vector.tensor_scalar(mask[:, v, :], c_i[:, :], quad_no[:, 0:1], None, ALU.is_equal)\
                    .then_inc(keyed, 1)
                dve.wait_ge(keyed, unit + 1)

            def one_hots(t, q):
                if not (isinstance(t, int) and t < 2):
                    dve.wait_ge(looked, t - 1)
                first, end = (0, HOTS) if q % 2 == 0 else (HOTS, PICKS)
                for a in range(first, end):
                    ins = nc.vector.tensor_scalar(hot[0:PU, q % 2, a - first, :], key[0:PU, :], float(QUADS * a), None,
                                                  ALU.is_equal)
                ins.then_inc(hot_made, 1)

            def early(t):
                dve.wait_ge(turned, turns(t, 0))
                lay(nc.vector.tensor_copy, 0).then_inc(laid_dve, 1)

            def tile(t, q, g):
                last = is_last(t)
                dve.wait_ge(turned, last_turned(t))
                if not has_found(t):
                    lay(nc.vector.tensor_copy, 3).then_inc(laid_dve, 1)
                if not (isinstance(t, int) and t + 2 >= TILES):
                    table_index(t + 2, q % 2)
                for step in range(STEPS):
                    dve.wait_ge(prod_made, STEPS * t + step + 1)
                    move(nc.vector.tensor_copy, step, (0, 1)).then_inc(moved_dve, 1)
                if isinstance(t, int) and t == 0:
                    dve.wait_ge(mlp_in, DMA * MLP_LOADS)
                dve.wait_ge(h0_summed, t + 1)
                for h in range(HALVES):
                    ins = nc.vector.tensor_scalar(hidden0[:, h, :], h0[h], lb_col[:, h:h + 1], 0.0, ALU.add, ALU.max)
                ins.then_inc(hidden0_dve, 1)
                dve.wait_ge(h1_summed, t + 1)
                nc.vector.tensor_scalar(hidden1[:, :], h1, b1_col[:, 0:1], 0.0, ALU.add, ALU.max)\
                    .then_inc(hidden1_made, 1)
                if last:
                    return
                early(t + 1)
                if isinstance(t, int) and t == 0:
                    split(0, 2)
                    keys(0, GROUP, 0)
                    one_hots(0, 0)
                if looks(g) and q % 2 == 1:
                    if q == 1:
                        keys(1, t + 3, FOUND * g + 1)
                    else:
                        keys(0, t + 1 + GROUP, FOUND * (g + 1))
                    dve.wait_ge(looked, t + 1)
                    nc.vector.tensor_tensor(picked[:, q // 2, :], ps_look[:, :], mask[:, q // 2, :], ALU.mult)\
                        .then_inc(masked, 1)
                if looks(g) and q == GROUP - 1:
                    dve.wait_ge(folded, g + 1)
                    nc.vector.tensor_copy(found[:, :], ps_look[0:FOUND * E, :]).then_inc(found_made, 1)
                    dve.wait_ge(found_made, g + 1)
                if has_found(t + 1):
                    home_q = (q + 1) % GROUP
                    lay(nc.vector.tensor_copy, 3, found[:, home_q * P:(home_q + 1) * P]).then_inc(laid_dve, 1)
                if looks(g):
                    one_hots(t + 1, q + 1)
                if isinstance(t, int) and t < PARTS - 1:
                    split(1, t + 1)

            early(0)
            split(0, 1)
            over_tiles(dve, tile)

        @block.scalar
        def _(act):
            def split(v, part):
                if part == 0:
                    act.wait_ge(table_loaded[v], DMA * 2)
                else:
                    act.wait_ge(part_dve, (PARTS - 1) * v + part)
                nc.scalar.copy(parts[0:PU, v, part, :], table_in[0:PU, v, :]).then_inc(part_act, 1)
            act.wait_ge(zeros_made, 2)

            def early(t):
                act.wait_ge(turned, turns(t, 1))
                lay(nc.scalar.copy, 1).then_inc(laid_act, 1)

            def tile(t, q, g):
                act.wait_ge(turned, turns(t, 2))
                lay(nc.scalar.copy, 2).then_inc(laid_act, 1)
                for step in range(STEPS):
                    act.wait_ge(prod_made, STEPS * t + step + 1)
                    move(nc.scalar.copy, step, (2, 3)).then_inc(moved_act, 1)
                if isinstance(t, int) and t == 0:
                    split(0, 1)
                    act.wait_ge(mlp_in, DMA * MLP_LOADS)
                act.wait_ge(logit_made, t + 1)
                nc.scalar.activation(scores[:, :].rearrange("o (b t) -> o t b", t=TILES)[:, bass.ds(t, 1), :],
                                     logit.rearrange("o (t b) -> o t b", t=1), ACT.Sigmoid,
                                     bias=bf_one[:, 0:1]).then_inc(logit_free, 1)
                if not is_last(t):
                    early(t + 1)
                if isinstance(t, int) and t == 0:
                    split(1, 0)
                    split(1, 1)

            early(0)
            split(0, 0)
            over_tiles(act, tile)

        @block.tensor
        def _(pe):
            pe.sem_inc(rows_used, 2)
            pe.sem_inc(logit_free, 1)
            pe.wait_ge(ident_made, 1)
            pe.wait_ge(dense_loaded, DMA)
            for g in range(TILES // QUADS):
                ins = nc.tensor.transpose(ps_turn[:, 0, g * P:(g + 1) * P],
                                          dense_in[:, QUADS * g:QUADS * (g + 1), :].rearrange("p t d -> p (t d)"),
                                          ident[:, :])
            ins.then_inc(dense_turned, 1)
            pe.wait_ge(dense_made, 1)
            pe.wait_ge(zeros_made, 2)
            pe.wait_ge(wz_in, DMA * 2)

            def turn(t, s, pair, group):
                first, end, bank = GROUPS[group]
                for j in range(first, end):
                    pe.wait_ge(landed[s][j], DMA * chunk_fields(j) * (pair + 1))
                    ins = nc.tensor.transpose(ps_turn[:, bank, (j - first) * P:(j - first + 1) * P],
                                              rows[:, s, j * P:(j + 1) * P], ident[:, :])
                ins.then_inc(turned, 1)

            def linear_term(group):
                first, end, _ = GROUPS[group]
                for j in range(first, end):
                    rows_j = E * chunk_fields(j)
                    for h in range(HALVES):
                        nc.tensor.matmul(h0[h], wz[0:rows_j, j, h * P:(h + 1) * P], field_rows[0:rows_j, j, :],
                                         start=(j == 0 and h == 0), stop=False, skip_group_check=True)

            def products(t):
                for step in range(STEPS):
                    if step >= 2:
                        pe.wait_ge(moved_dve, STEPS * t + step - 1)
                        pe.wait_ge(moved_act, STEPS * t + step - 1)
                    for q in range(PER_STEP):
                        b0 = ROWS4 * (PER_STEP * step + q)
                        ins = nc.tensor.matmul(ps_prod[:, step % 2, q * P:q * P + ROWS4 * NF],
                                               fields[:, b0:b0 + ROWS4, :].rearrange("e b f -> e (b f)"),
                                               fields[:, b0:b0 + ROWS4, 0:NF], start=True, stop=True)
                    ins.then_inc(prod_made, 1)

            def keep_clock(n):
                for _ in range(n):
                    nc.tensor.matmul(ps_prod[:, 1, 0:P], ident[:, :], ident[:, :], start=True, stop=True)

            def turn_early(t, q, g):
                s, pair = q % 2, (GROUP // 2) * g + q // 2
                turn(t, s, pair, 0)
                turn(t, s, pair, 1)

            def turn_late(t, q, g):
                s, pair = q % 2, (GROUP // 2) * g + q // 2
                pe.wait_ge(laid_act, 2 * t + 1)
                if is_last(t):
                    keep_clock(WARM[0])
                turn(t, s, pair, 2)
                if is_last(t):
                    keep_clock(WARM[1])
                if not has_found(t):
                    pe.wait_ge(laid_dve, 2 * t + 1)
                    turn(t, s, pair, 3)

            def free_rows(t):
                pe.wait_ge(turned, last_turned(t))
                pe.sem_inc(rows_used, 1)

            def early(t):
                pe.wait_ge(logit_free, t + 1)
                pe.wait_ge(laid_dve, 2 * t + 1)
                linear_term(0)
                pe.wait_ge(laid_act, 2 * t + 1)
                linear_term(1)

            def spread_rows(unit):
                pe.wait_ge(diag_made, unit + 1)
                nc.tensor.matmul(ps_prod[:, 0, 0:BANK], ones[:, :], diag[:, :], start=True, stop=True)\
                    .then_inc(spread, 1)

            def fold(g):
                pe.wait_ge(masked, FOUND * (g + 1))
                for v in range(FOUND):
                    ins = nc.tensor.matmul(ps_look[:, :], home[:, v, :], picked[:, v, :],
                                           start=(v == 0), stop=(v == FOUND - 1))
                ins.then_inc(folded, 1)

            def tile(t, q, g):
                last = is_last(t)
                unit = FOUND * g + q // 2
                picks = iter(range(HOTS) if q % 2 == 0 else range(HOTS, PICKS)) if looks(g) else iter(())

                def look(n):
                    for _ in range(n):
                        a = next(picks, None)
                        if a is None:
                            return
                        if a in (0, HOTS):
                            pe.wait_ge(hot_made, t + 1)
                            if isinstance(t, int) and t in (0, 2):
                                pe.wait_ge(part_act, (PARTS - 1) * (q // 2 + 1))
                                pe.wait_ge(part_dve, (PARTS - 1) * (q // 2 + 1))
                        if a == 0 and not (isinstance(g, int) and g == 0 and q == 0):
                            pe.wait_ge(masked, unit)
                        for part in range(PARTS):
                            ins = nc.tensor.matmul(ps_look[:, :], parts[0:PU, q // 2, part, P * a:P * (a + 1)],
                                                   hot[0:PU, q % 2, a % HOTS, :], start=(a == 0 and part == 0),
                                                   stop=(a == PICKS - 1 and part == PARTS - 1))
                        if a in (HOTS - 1, PICKS - 1):
                            ins.then_inc(looked, 1)

                if isinstance(t, int) and (t == 0 or t > GROUP * (NG - 1)):
                    turn_late(t, q, g)
                    free_rows(t)
                pe.wait_ge(laid_act, 2 * t + 2)
                linear_term(2)
                pe.wait_ge(laid_dve, 2 * t + 2)
                if looks(g) and q % 2 == 0 and not (isinstance(t, int) and t == 0):
                    pe.wait_ge(spread_read, unit + 1)
                products(t)
                linear_term(3)
                first_tile = isinstance(t, int) and t == 0
                if first_tile:
                    pe.wait_ge(ones_made, 1)
                    pe.wait_ge(home_made, 2)
                    pe.wait_ge(wp_in, DMA * PER)
                    pe.wait_ge(mlp_in, DMA * MLP_LOADS)
                else:
                    look(2)
                pe.wait_ge(moved_dve, STEPS * (t + 1))
                pe.wait_ge(moved_act, STEPS * (t + 1))
                for j in range(CH):
                    used = Q * chunk_fields(j)
                    for h in range(HALVES):
                        ins = nc.tensor.matmul(h0[h], wp[0:used, j, h * P:(h + 1) * P], pairs[0:used, j, :],
                                               start=False, stop=(j == CH - 1), skip_group_check=True)
                ins.then_inc(h0_summed, 1)
                nc.tensor.matmul(h1, w1_dense[:, :], dense_T[:, bass.ds(t, 1), :].rearrange("d t b -> d (t b)"),
                                 start=True, stop=False)
                if not first_tile:
                    look(1)
                pe.wait_ge(hidden0_dve, t + 1)
                for h in range(HALVES):
                    ins = nc.tensor.matmul(h1, w1[:, h, :], hidden0[:, h, :], start=False, stop=(h == HALVES - 1))
                ins.then_inc(h1_summed, 1)
                if not first_tile:
                    look(1)
                pe.wait_ge(hidden1_made, t + 1)
                nc.tensor.matmul(logit, wf[:, :], hidden1[:, :], start=True, stop=True).then_inc(logit_made, 1)
                if last:
                    return
                q_next, g_next = (q + 1) % GROUP, g + 1 if q == GROUP - 1 else g
                turn_early(t + 1, q_next, g_next)
                if looks(g):
                    if first_tile:
                        spread_rows(0)
                    look(4)
                    if q % 2 == 1:
                        spread_rows(unit + 1)
                    turn_late(t + 1, q_next, g_next)
                    look(1)
                    free_rows(t + 1)
                    look(HOTS)
                early(t + 1)
                if looks(g) and q == GROUP - 1:
                    fold(g)

            turn_early(0, 0, 0)
            early(0)
            over_tiles(pe, tile)


_INS = ['r_dense_inputs', 'r_sparse_inputs', 'L0_rec_tables', 'L0_rec_w_z', 'L0_rec_w_p', 'L0_rec_l_b', 'L0_rec_W1',
        'L0_rec_b1', 'L0_rec_Wf', 'L0_rec_bf']


def kernel(**inputs):
    import numpy as _np
    import concourse.bacc as _bacc
    from concourse import mybir as _mybir
    from concourse.bass_utils import run_bass_kernel_spmd as _run

    nc = _bacc.Bacc("TRN2", target_bir_lowering=False, num_devices=1)
    arrays, args = {}, []
    for name in _INS:
        a = _np.ascontiguousarray(inputs[name])
        arrays[f"in_{name}"] = a
        args.append(nc.dram_tensor(f"in_{name}", a.shape, _mybir.dt.from_np(a.dtype), kind="ExternalInput").ap())
    batch = inputs['r_dense_inputs'].shape[0]
    args.append(nc.dram_tensor("out_0", (batch, 1), _mybir.dt.float32, kind="ExternalOutput").ap())
    pnn_kernel(nc, *args)
    r = _run(nc, [arrays], core_ids=[0])
    return r.results[0]["out_0"]
```

```python
from contextlib import ExitStack

import concourse.bass as bass
from concourse import mybir

F32 = mybir.dt.float32
I32 = mybir.dt.int32
U32 = mybir.dt.uint32
BF16 = mybir.dt.bfloat16
ALU = mybir.AluOpType
ACT = mybir.ActivationFunctionType
AX = mybir.AxisListType

P = 128
Q = 32
BANK = 512
DMA = 16


def pnn_kernel(nc, dense, sparse, tables, w_z, w_p, l_b, W1, b1, Wf, bf, out):
    BATCH, NF = sparse.shape
    ND = dense.shape[1]
    _, VOCAB, E = tables.shape
    H = w_z.shape[2]
    H1 = W1.shape[1]
    TILES = BATCH // P
    PER = P // E
    CH = (NF + PER - 1) // PER
    LAST = NF - PER * (CH - 1)
    HALVES = H // P
    QUADS = P // Q
    BANK_OF = [0, 1, 1, 0]
    EARLY = [(0, 2), (2, 4)]
    PAIRS = TILES // 2
    WIDE = 2 * P
    FOUND = LAST
    PARTS = 3
    PICKS = -(-VOCAB // (P * QUADS))
    BLOCKS = QUADS * PICKS
    PU = VOCAB // BLOCKS
    ROWS4 = QUADS
    PER_STEP = 8
    STEPS = P // (ROWS4 * PER_STEP)
    WARM = [8, 2, 20, 6]
    assert FOUND == 2 and QUADS * PICKS <= 256 and VOCAB % BLOCKS == 0
    assert E == Q and PER == QUADS and BATCH % (2 * P) == 0 and NF <= Q and ND <= Q and H1 == P

    table_rows = tables.rearrange("f v e -> (f v) e")

    def chunk_fields(j):
        return LAST if j == CH - 1 else PER

    def chunks_with(u):
        return CH if u < LAST else CH - 1

    with ExitStack() as ctx:
        def sb(name, shape, dt=F32):
            return ctx.enter_context(nc.sbuf_tensor(name, shape, dt))

        def ps(name, shape):
            return ctx.enter_context(nc.psum_tensor(name, shape, F32))

        def sem(name):
            return ctx.enter_context(nc.semaphore(name))

        raw = sb("raw", [P, TILES * NF], I32)
        bounded = sb("bounded", [P, TILES * NF])
        wrap = sb("wrap", [P, TILES * NF])
        field_start = sb("field_start", [P, NF], I32)
        ident = sb("ident", [P, P])
        dense_in = sb("dense_in", [P, TILES, Q])
        dense_T = sb("dense_T", [ND, TILES, P])
        wz = sb("wz", [P, CH, H])
        wp = sb("wp", [P, CH, H])
        w1 = sb("w1", [P, HALVES, H1])
        w1_dense = sb("w1_dense", [ND, H1])
        wf = sb("wf", [H1, 1])
        lb_col = sb("lb_col", [P, HALVES])
        b1_col = sb("b1_col", [H1, 1])
        bf_one = sb("bf_one", [1, 1])
        which = sb("which", [P, 2, NF], U32)
        rows = sb("rows", [P, 2, CH * P])
        field_rows = sb("field_rows", [P, CH, P])
        fields = sb("fields", [P, P, Q])
        pairs = sb("pairs", [P, CH, P])
        hidden0 = sb("hidden0", [P, HALVES, P])
        hidden1 = sb("hidden1", [H1, P])
        scores = sb("scores", [1, BATCH])
        table_in = sb("table_in", [P, FOUND, BLOCKS * E])
        parts = sb("parts", [P, FOUND, PARTS, BLOCKS * E], BF16)
        look_row = sb("look_row", [P, FOUND, TILES + 2])
        ones = sb("ones", [P, P])
        home = sb("home", [P, FOUND, P])
        part_i = sb("part_i", [P, 1], I32)
        before_i = sb("before_i", [P, 1], I32)
        quad_i = sb("quad_i", [P, 1], I32)
        before = sb("before", [P, 1])
        quad_no = sb("quad_no", [P, 1])
        diag = sb("diag", [P, WIDE])
        row_i = sb("row_i", [P, WIDE], I32)
        c_i = sb("c_i", [P, WIDE], I32)
        key = sb("key", [P, WIDE], BF16)
        mask = sb("mask", [P, FOUND, WIDE])
        hot = sb("hot", [P, FOUND, PICKS, WIDE], BF16)
        picked = sb("picked", [P, FOUND, WIDE])
        found = sb("found", [FOUND * E, WIDE])

        ps_turn = ps("ps_turn", [P, 2, BANK])
        ps_prod = ps("ps_prod", [P, 2, PER_STEP * P])
        ps_h0 = ps("ps_h0", [P, BANK])
        ps_look = ps("ps_look", [P, WIDE])
        h0 = [ps_h0[:, h * P:(h + 1) * P] for h in range(HALVES)]
        logit = ps_h0[0:1, HALVES * P:(HALVES + 1) * P]
        h1 = ps_turn[:, 1, 0:P]

        raw_in = sem("raw_in")
        rest_in = sem("rest_in")
        dense_loaded = sem("dense_loaded")
        wz_in = sem("wz_in")
        wp_in = sem("wp_in")
        mlp_in = sem("mlp_in")
        start_made = sem("start_made")
        ident_zero = sem("ident_zero")
        ident_made = sem("ident_made")
        wrap_made = sem("wrap_made")
        bounded_made = sem("bounded_made")
        zeros_made = sem("zeros_made")
        dense_turned = sem("dense_turned")
        dense_made = sem("dense_made")
        which_made = sem("which_made")
        landed = [[sem(f"landed_{s}_{j}") for j in range(CH)] for s in range(2)]
        rows_used = sem("rows_used")
        turned = sem("turned")
        laid_dve = sem("laid_dve")
        laid_group3 = sem("laid_group3")
        laid_found = sem("laid_found")
        laid_act = sem("laid_act")
        prod_made = sem("prod_made")
        moved_dve = sem("moved_dve")
        moved_act = sem("moved_act")
        h0_summed = sem("h0_summed")
        hidden0_dve = sem("hidden0_dve")
        h1_summed = sem("h1_summed")
        hidden1_made = sem("hidden1_made")
        logit_made = sem("logit_made")
        logit_free = sem("logit_free")
        stored = sem("stored")
        table_loaded = [sem(f"table_loaded_{v}") for v in range(FOUND)]
        part_numbered = sem("part_numbered")
        numbers_made = sem("numbers_made")
        rows_clipped = sem("rows_clipped")
        ones_made = sem("ones_made")
        home_made = sem("home_made")
        part_act = sem("part_act")
        part_dve = sem("part_dve")
        diag_made = sem("diag_made")
        spread = sem("spread")
        spread_read = sem("spread_read")
        row_cut = sem("row_cut")
        keyed = sem("keyed")
        hot_made = sem("hot_made")
        looked = sem("looked")
        masked = sem("masked")
        folded = sem("folded")
        found_made = sem("found_made")

        def over_tiles(eng, tile):
            for s in range(2):
                tile(s, s, 0)
            with eng.Fori(1, PAIRS - 1) as pair:
                for s in range(2):
                    tile(2 * pair + s, s, pair)
            for s in range(2):
                tile(TILES - 2 + s, s, PAIRS - 1)

        def at(t, *tiles):
            return isinstance(t, int) and t in tiles

        def is_last(t):
            return at(t, TILES - 1)

        def looks(t):
            return not at(t, TILES - 2, TILES - 1)

        def has_found(t):
            return not at(t, 0, 1)

        def chunks(t, group):
            if group < 2:
                return EARLY[group]
            gathered = CH - 1 if has_found(t) else CH
            late = gathered - 1 if has_group3(t) else gathered
            return (EARLY[1][1], late) if group == 2 else (late, gathered)

        def has_group3(t):
            return at(t, 0, 1, TILES - 1)

        def turns(t, group):
            return 3 * t + group + 1 + (min(t, 2) if isinstance(t, int) else 2)

        def last_turned(t):
            return turns(t, 3 if has_group3(t) else 2)

        def laid_3(t):
            return 3 if is_last(t) else t + 1

        def lay(copy, first, end, turned_rows):
            used = turned_rows.shape[0]
            copy(field_rows[0:used, first:end, :], turned_rows.rearrange("p (j b) -> p j b", b=P))
            for u in range(PER):
                n = min(end, chunks_with(u)) - first
                if n > 0:
                    src = turned_rows[Q * u:Q * (u + 1), 0:n * P].rearrange("e (j b) -> e b j", b=P)
                    ins = copy(fields[0:E, :, PER * first + u:PER * (first + n - 1) + u + 1:PER], src)
            return ins

        def lay_group(copy, t, group):
            first, end = chunks(t, group)
            return lay(copy, first, end, ps_turn[:, BANK_OF[group], 0:(end - first) * P])

        def move(copy, step, rows4):
            b0 = step * PER_STEP * ROWS4
            for c in rows4:
                for k in range(PER):
                    n = chunks_with(k)
                    src = ps_prod[Q * c:Q * (c + 1), step % 2, :].rearrange("f (q g) -> f q g", g=P)[
                        :, :, NF * c + k:NF * c + k + PER * (n - 1) + 1:PER]
                    dst = pairs[Q * k:Q * (k + 1), 0:n, b0 + c:b0 + c + ROWS4 * (PER_STEP - 1) + 1:ROWS4]
                    ins = copy(dst.rearrange("f j q -> f q j"), src)
            return ins

        block = ctx.enter_context(nc.Block())

        @block.sync
        def _(sp):
            indices = sparse.rearrange("(p t) f -> p (t f)", t=TILES)
            sp.dma_start(raw[:, 0:2 * NF], indices[:, 0:2 * NF]).then_inc(raw_in, DMA)
            sp.dma_start(raw[:, 2 * NF:TILES * NF], indices[:, 2 * NF:TILES * NF]).then_inc(rest_in, DMA)
            sp.wait_ge(zeros_made, 1)
            sp.dma_start(dense_in[:, :, 0:ND], dense.rearrange("(p t) d -> p t d", t=TILES)).then_inc(dense_loaded, DMA)
            wz_rows = w_z.rearrange("f e h -> (f e) h")
            sp.dma_start(wz[:, 0:CH - 1, :], wz_rows[0:(CH - 1) * P, :].rearrange("(j p) h -> p j h", p=P))\
                .then_inc(wz_in, DMA)
            sp.dma_start(wz[0:LAST * E, CH - 1, :], wz_rows[(CH - 1) * P:, :]).then_inc(wz_in, DMA)
            for k in range(PER):
                n = chunks_with(k)
                sp.dma_start(wp[Q * k:Q * k + NF, 0:n, :], w_p[:, k:k + PER * (n - 1) + 1:PER, :]).then_inc(wp_in, DMA)
            sp.dma_start(w1[:, :, :], W1[0:H, :].rearrange("(c p) n -> p c n", p=P)).then_inc(mlp_in, DMA)
            sp.dma_start(w1_dense[:, :], W1[H:H + ND, :]).then_inc(mlp_in, DMA)
            sp.dma_start(wf[:, :], Wf[:, :]).then_inc(mlp_in, DMA)
            with nc.allow_non_contiguous_dma(reason="bias columns, a few hundred values"):
                sp.dma_start(lb_col[:, :], l_b.rearrange("(c p) -> p c", p=P)).then_inc(mlp_in, DMA)
                sp.dma_start(b1_col[:, :], b1.rearrange("(p o) -> p o", o=1)).then_inc(mlp_in, DMA)
            sp.dma_start(bf_one[:, :], bf.rearrange("(p o) -> p o", o=1)).then_inc(mlp_in, DMA)
            half_row = BLOCKS * E // 2
            for v in range(FOUND):
                table = tables[NF - FOUND + v].rearrange("(l r) e -> l (r e)", l=PU)
                for half in range(2):
                    after = FOUND * v + half
                    sp.wait_ge(landed[0][after], DMA * PER)
                    sp.dma_start(table_in[0:PU, v, half_row * half:half_row * (half + 1)],
                                 table[:, half_row * half:half_row * (half + 1)]).then_inc(table_loaded[v], DMA)
            sp.wait_ge(logit_free, TILES + 1)
            sp.dma_start(out.rearrange("b o -> o b"), scores[:, :]).then_inc(stored, DMA)
            sp.wait_ge(stored, DMA)

        MLP_LOADS = 6
        CUTS = (8, 12)
        LOOKS = (2, 3, 2)

        @block.gpsimd
        def _(pool):
            nc.gpsimd.iota(field_start[:, :], pattern=[[VOCAB, NF]], base=0, channel_multiplier=0)\
                .then_inc(start_made, 1)
            nc.gpsimd.iota(part_i[:, :], pattern=[[0, 1]], base=0, channel_multiplier=1)
            nc.gpsimd.iota(before_i[:, :], pattern=[[0, 1]], base=0, channel_multiplier=-BLOCKS).then_inc(part_numbered, 1)
            nc.gpsimd.memset(ident[:, :], 0.0).then_inc(ident_zero, 1)
            pool.wait_ge(ident_zero, 1)
            nc.gpsimd.affine_select(out=ident[:, :], in_=ident[:, :], compare_op=ALU.not_equal, fill=1.0, base=0,
                                    pattern=[[-1, P]], channel_multiplier=1).then_inc(ident_made, 1)

            def gather(t, s, pair):
                pool.wait_ge(which_made, t + 1)
                pool.wait_ge(rows_used, t + 1)
                pool.nop(nofuse=True)
                for f in range(NF - FOUND if has_found(t) else NF):
                    nc.gpsimd.indirect_dma_start(
                        rows[:, s, E * f:E * (f + 1)], None, table_rows,
                        bass.IndirectOffsetOnAxis(ap=which[:, s, f:f + 1], axis=0),
                    ).then_inc(landed[s][f // PER], DMA)

            over_tiles(pool, gather)

        @block.vector
        def _(dve):
            def bound_indices(tiles):
                cols = slice(NF * tiles[0], NF * tiles[1])
                n = 1 if tiles[0] == 0 else 2
                nc.vector.tensor_scalar(wrap[:, cols], raw[:, cols], 0.0, float(VOCAB), ALU.is_lt, ALU.mult)\
                    .then_inc(wrap_made, 1)
                dve.wait_ge(wrap_made, n)
                nc.vector.scalar_tensor_tensor(out=bounded[:, cols], in0=raw[:, cols], scalar=float(VOCAB - 1),
                                               in1=wrap[:, cols], op0=ALU.min, op1=ALU.add).then_inc(bounded_made, 1)
                dve.wait_ge(bounded_made, n)

            def table_index(t, s):
                nc.vector.scalar_tensor_tensor(out=which[:, s, :], in0=bounded[:, bass.ds(t * NF, NF)], scalar=0.0,
                                               in1=field_start[:, :], op0=ALU.max, op1=ALU.add).then_inc(which_made, 1)

            dve.wait_ge(raw_in, DMA)
            bound_indices((0, 2))
            dve.wait_ge(start_made, 1)
            table_index(0, 0)
            table_index(1, 1)
            nc.vector.memset(dense_in[:, :, :], 0.0)
            nc.vector.memset(wp[:, :, :], 0.0).then_inc(zeros_made, 1)
            dve.wait_ge(rest_in, DMA)
            bound_indices((2, TILES))
            nc.vector.memset(rows[:, :, NF * E:CH * P], 0.0)
            nc.vector.memset(fields[:, :, :], 0.0).then_inc(zeros_made, 1)
            dve.wait_ge(dense_turned, 1)
            for u in range(QUADS):
                ins = nc.vector.tensor_scalar(dense_T[:, u:TILES:QUADS, :],
                                              ps_turn[Q * u:Q * u + ND, 0, :].rearrange("d (g b) -> d g b", b=P),
                                              0.0, None, ALU.max)
            ins.then_inc(dense_made, 1)
            dve.wait_ge(part_numbered, 1)
            nc.vector.tensor_copy(before[:, :], before_i[:, :])
            nc.vector.tensor_scalar(quad_i[:, :], part_i[:, :], Q.bit_length() - 1, None, ALU.logical_shift_right)\
                .then_inc(numbers_made, 1)
            dve.wait_ge(numbers_made, 1)
            nc.vector.tensor_copy(quad_no[:, :], quad_i[:, :]).then_inc(numbers_made, 1)
            nc.vector.memset(look_row[:, :, TILES:TILES + 2], 0.0)
            nc.vector.tensor_scalar(look_row[:, :, 0:TILES],
                                    bounded[:, :].rearrange("p (t f) -> p f t", f=NF)[:, NF - FOUND:NF, :],
                                    0.0, None, ALU.max).then_inc(rows_clipped, 1)
            nc.vector.memset(ones[:, :], 1.0).then_inc(ones_made, 1)
            nc.vector.memset(home[:, :, :], 0.0).then_inc(home_made, 1)
            dve.wait_ge(ident_made, 1)
            dve.wait_ge(home_made, 1)
            for v in range(FOUND):
                ins = nc.vector.tensor_reduce(home[:, v, E * v:E * (v + 1)],
                                              ident[:, :].rearrange("p (c e) -> p e c", c=QUADS), AX.X, ALU.add)
            ins.then_inc(home_made, 1)

            def split(v, part):
                dve.wait_ge(part_act, (PARTS - 1) * v + part)
                rest = table_in[0:PU, v, :] if part < PARTS - 1 else parts[0:PU, v, part, :]
                nc.vector.tensor_tensor(rest, table_in[0:PU, v, :], parts[0:PU, v, part - 1, :], ALU.subtract)\
                    .then_inc(part_dve, 1)

            dve.wait_ge(rows_clipped, 1)
            dve.wait_ge(numbers_made, 2)

            def diagonal(v, target):
                for k in range(2):
                    ins = nc.vector.tensor_scalar(diag[:, k * P:(k + 1) * P], ident[:, :],
                                                  look_row[:, v, bass.ds(target + k, 1)], None, ALU.mult)
                ins.then_inc(diag_made, 1)

            def keys(v, unit):
                dve.wait_ge(spread, unit + 1)
                nc.vector.tensor_copy(row_i[:, :], ps_prod[:, 0, 0:WIDE]).then_inc(spread_read, 1)
                dve.wait_ge(spread_read, unit + 1)
                nc.vector.tensor_scalar(c_i[:, :], row_i[:, :], QUADS - 1, None, ALU.bitwise_and).then_inc(row_cut, 1)
                dve.wait_ge(row_cut, unit + 1)
                nc.vector.scalar_tensor_tensor(out=key[0:PU, :], in0=row_i[0:PU, :], scalar=before[0:PU, 0:1],
                                               in1=c_i[0:PU, :], op0=ALU.add, op1=ALU.subtract)
                nc.vector.tensor_scalar(mask[:, v, :], c_i[:, :], quad_no[:, 0:1], None, ALU.is_equal)\
                    .then_inc(keyed, 1)
                dve.wait_ge(keyed, unit + 1)

            def one_hots(v, first, end):
                for a in range(first, end):
                    ins = nc.vector.tensor_scalar(hot[0:PU, v, a, :], key[0:PU, :], float(QUADS * a), None, ALU.is_equal)
                if end == PICKS:
                    ins.then_inc(hot_made, 1)

            def early(t):
                dve.wait_ge(turned, turns(t, 0))
                lay_group(nc.vector.tensor_copy, t, 0).then_inc(laid_dve, 1)

            def tile(t, s, pair):
                v_next = 1 - s
                target = 2 * (pair + s) + 2
                dve.wait_ge(turned, last_turned(t))
                if has_group3(t):
                    lay_group(nc.vector.tensor_copy, t, 3).then_inc(laid_group3, 1)
                if not at(t, TILES - 2, TILES - 1):
                    table_index(t + 2, s)
                if looks(t):
                    diagonal(v_next, target)
                if at(t, 0):
                    split(0, 2)
                for step in range(STEPS):
                    dve.wait_ge(prod_made, STEPS * t + step + 1)
                    move(nc.vector.tensor_copy, step, (0, 1)).then_inc(moved_dve, 1)
                if looks(t):
                    keys(v_next, t + 1)
                    one_hots(v_next, 0, CUTS[0])
                if at(t, 0):
                    dve.wait_ge(mlp_in, DMA * MLP_LOADS)
                dve.wait_ge(h0_summed, t + 1)
                for h in range(HALVES):
                    ins = nc.vector.tensor_scalar(hidden0[:, h, :], h0[h], lb_col[:, h:h + 1], 0.0, ALU.add, ALU.max)
                ins.then_inc(hidden0_dve, 1)
                if looks(t):
                    one_hots(v_next, CUTS[0], CUTS[1])
                dve.wait_ge(h1_summed, t + 1)
                nc.vector.tensor_scalar(hidden1[:, :], h1, b1_col[:, 0:1], 0.0, ALU.add, ALU.max)\
                    .then_inc(hidden1_made, 1)
                if is_last(t):
                    return
                early(t + 1)
                if has_found(t) and s == 0:
                    lay(nc.vector.tensor_copy, CH - 1, CH, found[:, P:2 * P]).then_inc(laid_found, 1)
                if looks(t):
                    one_hots(v_next, CUTS[1], PICKS)
                    if at(t, 0):
                        split(1, 1)
                    dve.wait_ge(looked, t + 1)
                    nc.vector.tensor_tensor(picked[:, s, :], ps_look[:, :], mask[:, s, :], ALU.mult)\
                        .then_inc(masked, 1)
                    if at(t, 0):
                        split(1, 2)
                if looks(t) and s == 1:
                    dve.wait_ge(folded, pair + 1)
                    nc.vector.tensor_copy(found[:, :], ps_look[0:FOUND * E, :]).then_inc(found_made, 1)
                    dve.wait_ge(found_made, pair + 1)
                    lay(nc.vector.tensor_copy, CH - 1, CH, found[:, 0:P]).then_inc(laid_found, 1)

            diagonal(0, 2)
            early(0)
            keys(0, 0)
            one_hots(0, 0, PICKS)
            split(0, 1)
            over_tiles(dve, tile)

        @block.scalar
        def _(act):
            def split(v, part):
                if part == 0:
                    act.wait_ge(table_loaded[v], DMA * 2)
                else:
                    act.wait_ge(part_dve, (PARTS - 1) * v + part)
                nc.scalar.copy(parts[0:PU, v, part, :], table_in[0:PU, v, :]).then_inc(part_act, 1)

            act.wait_ge(zeros_made, 2)

            def early(t):
                act.wait_ge(turned, turns(t, 1))
                lay_group(nc.scalar.copy, t, 1).then_inc(laid_act, 1)

            def tile(t, s, pair):
                act.wait_ge(turned, turns(t, 2))
                lay_group(nc.scalar.copy, t, 2).then_inc(laid_act, 1)
                if at(t, 0):
                    split(0, 1)
                for step in range(STEPS):
                    act.wait_ge(prod_made, STEPS * t + step + 1)
                    move(nc.scalar.copy, step, (2, 3)).then_inc(moved_act, 1)
                if at(t, 0):
                    split(1, 0)
                    act.wait_ge(mlp_in, DMA * MLP_LOADS)
                act.wait_ge(logit_made, t + 1)
                nc.scalar.activation(scores[:, :].rearrange("o (b t) -> o t b", t=TILES)[:, bass.ds(t, 1), :],
                                     logit.rearrange("o (t b) -> o t b", t=1), ACT.Sigmoid,
                                     bias=bf_one[:, 0:1]).then_inc(logit_free, 1)
                if not is_last(t):
                    early(t + 1)
                if at(t, 0):
                    split(1, 1)

            early(0)
            split(0, 0)
            over_tiles(act, tile)

        @block.tensor
        def _(pe):
            pe.sem_inc(rows_used, 2)
            pe.sem_inc(logit_free, 1)
            pe.wait_ge(ident_made, 1)
            pe.wait_ge(dense_loaded, DMA)
            for g in range(TILES // QUADS):
                ins = nc.tensor.transpose(ps_turn[:, 0, g * P:(g + 1) * P],
                                          dense_in[:, QUADS * g:QUADS * (g + 1), :].rearrange("p t d -> p (t d)"),
                                          ident[:, :])
            ins.then_inc(dense_turned, 1)
            pe.wait_ge(dense_made, 1)
            pe.wait_ge(zeros_made, 2)
            pe.wait_ge(wz_in, DMA * 2)

            def turn(t, s, pair, group):
                first, end = chunks(t, group)
                for j in range(first, end):
                    pe.wait_ge(landed[s][j], DMA * chunk_fields(j) * (pair + 1))
                    ins = nc.tensor.transpose(ps_turn[:, BANK_OF[group], (j - first) * P:(j - first + 1) * P],
                                              rows[:, s, j * P:(j + 1) * P], ident[:, :])
                ins.then_inc(turned, 1)

            def linear_term(first, end):
                for j in range(first, end):
                    rows_j = E * chunk_fields(j)
                    for h in range(HALVES):
                        nc.tensor.matmul(h0[h], wz[0:rows_j, j, h * P:(h + 1) * P], field_rows[0:rows_j, j, :],
                                         start=(j == 0 and h == 0), stop=False, skip_group_check=True)

            def products(t):
                for step in range(STEPS):
                    if step >= 2:
                        pe.wait_ge(moved_dve, STEPS * t + step - 1)
                        pe.wait_ge(moved_act, STEPS * t + step - 1)
                    for q in range(PER_STEP):
                        b0 = ROWS4 * (PER_STEP * step + q)
                        ins = nc.tensor.matmul(ps_prod[:, step % 2, q * P:q * P + ROWS4 * NF],
                                               fields[:, b0:b0 + ROWS4, :].rearrange("e b f -> e (b f)"),
                                               fields[:, b0:b0 + ROWS4, 0:NF], start=True, stop=True)
                    ins.then_inc(prod_made, 1)

            def keep_clock(n):
                for _ in range(n):
                    nc.tensor.matmul(ps_prod[:, 1, 0:P], ident[:, :], ident[:, :], start=True, stop=True)

            def turn_early(t, s, pair):
                turn(t, s, pair, 0)
                turn(t, s, pair, 1)

            def turn_late(t, s, pair):
                pe.wait_ge(laid_act, 2 * t + 1)
                if is_last(t):
                    keep_clock(WARM[1])
                turn(t, s, pair, 2)
                if is_last(t):
                    keep_clock(WARM[2])
                if has_group3(t):
                    pe.wait_ge(laid_dve, t + 1)
                    turn(t, s, pair, 3)
                if is_last(t):
                    keep_clock(WARM[3])

            def free_rows(t):
                pe.wait_ge(turned, last_turned(t))
                pe.sem_inc(rows_used, 1)

            def linear_0(t):
                pe.wait_ge(logit_free, t + 1)
                pe.wait_ge(laid_dve, t + 1)
                linear_term(0, 2)

            def linear_1(t):
                pe.wait_ge(laid_act, 2 * t + 1)
                linear_term(2, 4)

            def spread_rows(unit):
                pe.wait_ge(diag_made, unit + 1)
                nc.tensor.matmul(ps_prod[:, 0, 0:WIDE], ones[:, :], diag[:, :], start=True, stop=True)\
                    .then_inc(spread, 1)

            def fold(pair):
                pe.wait_ge(masked, FOUND * (pair + 1))
                for v in range(FOUND):
                    ins = nc.tensor.matmul(ps_look[:, :], home[:, v, :], picked[:, v, :],
                                           start=(v == 0), stop=(v == FOUND - 1))
                ins.then_inc(folded, 1)

            def tile(t, s, pair):
                picks = iter(range(PICKS) if looks(t) else ())

                def look(n):
                    for _ in range(n):
                        a = next(picks, None)
                        if a is None:
                            return
                        if a == 0:
                            pe.wait_ge(hot_made, t + 1)
                            if at(t, 0, 1):
                                pe.wait_ge(part_act, (PARTS - 1) * (s + 1))
                                pe.wait_ge(part_dve, (PARTS - 1) * (s + 1))
                            if not at(t, 0):
                                pe.wait_ge(masked, t)
                        for part in range(PARTS):
                            ins = nc.tensor.matmul(ps_look[:, :], parts[0:PU, s, part, P * a:P * (a + 1)],
                                                   hot[0:PU, s, a, :], start=(a == 0 and part == 0),
                                                   stop=(a == PICKS - 1 and part == PARTS - 1))
                        if a == PICKS - 1:
                            ins.then_inc(looked, 1)

                if at(t, 0, TILES - 1):
                    turn_late(t, s, pair)
                    free_rows(t)
                pe.wait_ge(laid_act, 2 * t + 2)
                first, end = chunks(t, 2)
                late = first if is_last(t) else end
                linear_term(first, late)
                if has_group3(t):
                    pe.wait_ge(laid_group3, laid_3(t))
                if has_found(t):
                    pe.wait_ge(laid_found, t - 1)
                if not is_last(t):
                    pe.wait_ge(spread_read, t + 1)
                products(t)
                linear_term(late, CH)
                if at(t, 0):
                    pe.wait_ge(home_made, 2)
                    pe.wait_ge(wp_in, DMA * PER)
                    pe.wait_ge(mlp_in, DMA * MLP_LOADS)
                look(LOOKS[0])
                pe.wait_ge(moved_dve, STEPS * (t + 1))
                pe.wait_ge(moved_act, STEPS * (t + 1))
                if looks(t):
                    spread_rows(t + 1)
                for j in range(CH):
                    used = Q * chunk_fields(j)
                    for h in range(HALVES):
                        ins = nc.tensor.matmul(h0[h], wp[0:used, j, h * P:(h + 1) * P], pairs[0:used, j, :],
                                               start=False, stop=(j == CH - 1), skip_group_check=True)
                ins.then_inc(h0_summed, 1)
                nc.tensor.matmul(h1, w1_dense[:, :], dense_T[:, bass.ds(t, 1), :].rearrange("d t b -> d (t b)"),
                                 start=True, stop=False)
                look(LOOKS[1])
                pe.wait_ge(hidden0_dve, t + 1)
                for h in range(HALVES):
                    ins = nc.tensor.matmul(h1, w1[:, h, :], hidden0[:, h, :], start=False, stop=(h == HALVES - 1))
                ins.then_inc(h1_summed, 1)
                look(LOOKS[2])
                pe.wait_ge(hidden1_made, t + 1)
                nc.tensor.matmul(logit, wf[:, :], hidden1[:, :], start=True, stop=True).then_inc(logit_made, 1)
                if is_last(t):
                    return
                s_next, pair_next = 1 - s, pair + s
                turn_early(t + 1, s_next, pair_next)
                if looks(t):
                    look(PICKS)
                    turn_late(t + 1, s_next, pair_next)
                    linear_0(t + 1)
                    if s == 1:
                        fold(pair)
                    free_rows(t + 1)
                else:
                    keep_clock(WARM[0])
                    linear_0(t + 1)
                linear_1(t + 1)

            turn_early(0, 0, 0)
            pe.wait_ge(ones_made, 1)
            spread_rows(0)
            linear_0(0)
            linear_1(0)
            over_tiles(pe, tile)


_INS = ['r_dense_inputs', 'r_sparse_inputs', 'L0_rec_tables', 'L0_rec_w_z', 'L0_rec_w_p', 'L0_rec_l_b', 'L0_rec_W1',
        'L0_rec_b1', 'L0_rec_Wf', 'L0_rec_bf']


def kernel(**inputs):
    import numpy as _np
    import concourse.bacc as _bacc
    from concourse import mybir as _mybir
    from concourse.bass_utils import run_bass_kernel_spmd as _run

    nc = _bacc.Bacc("TRN2", target_bir_lowering=False, num_devices=1)
    arrays, args = {}, []
    for name in _INS:
        a = _np.ascontiguousarray(inputs[name])
        arrays[f"in_{name}"] = a
        args.append(nc.dram_tensor(f"in_{name}", a.shape, _mybir.dt.from_np(a.dtype), kind="ExternalInput").ap())
    batch = inputs['r_dense_inputs'].shape[0]
    args.append(nc.dram_tensor("out_0", (batch, 1), _mybir.dt.float32, kind="ExternalOutput").ap())
    pnn_kernel(nc, *args)
    r = _run(nc, [arrays], core_ids=[0])
    return r.results[0]["out_0"]
```
